# Optimizing a Trainium2 kernel written in Bass

```python
import numpy as np
import jax
import jax.numpy as jnp

def _softmax(x, axis=-1):
    return jax.nn.softmax(x, axis=axis)

def _gelu(x):
    return jax.nn.gelu(x, approximate=True)

def _silu(x):
    return jax.nn.silu(x)

def _sigmoid(x):
    return jax.nn.sigmoid(x)

def _layernorm(x, axis=-1, eps=1e-05):
    m = jnp.mean(x, axis=axis, keepdims=True)
    v = jnp.var(x, axis=axis, keepdims=True)
    return (x - m) / jnp.sqrt(v + eps)

def _scatter_add(tgt, idx, src, axis=0):
    return tgt.at[idx].add(src)

def _segment_sum(src, seg, n):
    return jax.ops.segment_sum(src, seg, n)
kernel_name = 'mk_dlrm_tower_d1_rec_r8_cc7332'

def setup_inputs(seed: int=0):
    np.random.seed(seed)
    _w = jnp.asarray

    def _rec_inputs():
        import jax
        import jax.numpy as jnp
        _tk = jax.random.key(seed)
        dense_ctx = jax.random.normal(jax.random.fold_in(_tk, 190), (512, 16), jnp.float32)
        ids = jnp.stack([jax.random.randint(jax.random.fold_in(_tk, 200 + f), (512,), 0, v, jnp.int32) for f, v in enumerate([125000, 1000, 12500, 1000, 1250, 12500, 12500, 1000, 12500, 125000, 1250, 1250, 12500, 1250, 1000, 1000, 1250, 125000, 12500, 1000, 1000, 1250, 1250, 12500, 12500, 1250, 1000, 1000, 1000, 1000, 1250, 1000])], axis=1)
        tbl_0 = 0.05 * jax.random.normal(jax.random.fold_in(_tk, 500 + 0), (125000, 64), jnp.float32)
        tbl_1 = 0.05 * jax.random.normal(jax.random.fold_in(_tk, 500 + 1), (1000, 64), jnp.float32)
        tbl_2 = 0.05 * jax.random.normal(jax.random.fold_in(_tk, 500 + 2), (12500, 64), jnp.float32)
        tbl_3 = 0.05 * jax.random.normal(jax.random.fold_in(_tk, 500 + 3), (1000, 64), jnp.float32)
        tbl_4 = 0.05 * jax.random.normal(jax.random.fold_in(_tk, 500 + 4), (1250, 64), jnp.float32)
        tbl_5 = 0.05 * jax.random.normal(jax.random.fold_in(_tk, 500 + 5), (12500, 64), jnp.float32)
        tbl_6 = 0.05 * jax.random.normal(jax.random.fold_in(_tk, 500 + 6), (12500, 64), jnp.float32)
        tbl_7 = 0.05 * jax.random.normal(jax.random.fold_in(_tk, 500 + 7), (1000, 64), jnp.float32)
        tbl_8 = 0.05 * jax.random.normal(jax.random.fold_in(_tk, 500 + 8), (12500, 64), jnp.float32)
        tbl_9 = 0.05 * jax.random.normal(jax.random.fold_in(_tk, 500 + 9), (125000, 64), jnp.float32)
        tbl_10 = 0.05 * jax.random.normal(jax.random.fold_in(_tk, 500 + 10), (1250, 64), jnp.float32)
        tbl_11 = 0.05 * jax.random.normal(jax.random.fold_in(_tk, 500 + 11), (1250, 64), jnp.float32)
        tbl_12 = 0.05 * jax.random.normal(jax.random.fold_in(_tk, 500 + 12), (12500, 64), jnp.float32)
        tbl_13 = 0.05 * jax.random.normal(jax.random.fold_in(_tk, 500 + 13), (1250, 64), jnp.float32)
        tbl_14 = 0.05 * jax.random.normal(jax.random.fold_in(_tk, 500 + 14), (1000, 64), jnp.float32)
        tbl_15 = 0.05 * jax.random.normal(jax.random.fold_in(_tk, 500 + 15), (1000, 64), jnp.float32)
        tbl_16 = 0.05 * jax.random.normal(jax.random.fold_in(_tk, 500 + 16), (1250, 64), jnp.float32)
        tbl_17 = 0.05 * jax.random.normal(jax.random.fold_in(_tk, 500 + 17), (125000, 64), jnp.float32)
        tbl_18 = 0.05 * jax.random.normal(jax.random.fold_in(_tk, 500 + 18), (12500, 64), jnp.float32)
        tbl_19 = 0.05 * jax.random.normal(jax.random.fold_in(_tk, 500 + 19), (1000, 64), jnp.float32)
        tbl_20 = 0.05 * jax.random.normal(jax.random.fold_in(_tk, 500 + 20), (1000, 64), jnp.float32)
        tbl_21 = 0.05 * jax.random.normal(jax.random.fold_in(_tk, 500 + 21), (1250, 64), jnp.float32)
        tbl_22 = 0.05 * jax.random.normal(jax.random.fold_in(_tk, 500 + 22), (1250, 64), jnp.float32)
        tbl_23 = 0.05 * jax.random.normal(jax.random.fold_in(_tk, 500 + 23), (12500, 64), jnp.float32)
        tbl_24 = 0.05 * jax.random.normal(jax.random.fold_in(_tk, 500 + 24), (12500, 64), jnp.float32)
        tbl_25 = 0.05 * jax.random.normal(jax.random.fold_in(_tk, 500 + 25), (1250, 64), jnp.float32)
        tbl_26 = 0.05 * jax.random.normal(jax.random.fold_in(_tk, 500 + 26), (1000, 64), jnp.float32)
        tbl_27 = 0.05 * jax.random.normal(jax.random.fold_in(_tk, 500 + 27), (1000, 64), jnp.float32)
        tbl_28 = 0.05 * jax.random.normal(jax.random.fold_in(_tk, 500 + 28), (1000, 64), jnp.float32)
        tbl_29 = 0.05 * jax.random.normal(jax.random.fold_in(_tk, 500 + 29), (1000, 64), jnp.float32)
        tbl_30 = 0.05 * jax.random.normal(jax.random.fold_in(_tk, 500 + 30), (1250, 64), jnp.float32)
        tbl_31 = 0.05 * jax.random.normal(jax.random.fold_in(_tk, 500 + 31), (1000, 64), jnp.float32)
        _rk = jax.random.fold_in(_tk, 7)
        W_top1 = 0.0441942 * jax.random.normal(jax.random.fold_in(_tk, 801), (512, 512), jnp.float32)
        W_top2 = 0.0441942 * jax.random.normal(jax.random.fold_in(_tk, 802), (512, 256), jnp.float32)
        W_top3 = 0.0625 * jax.random.normal(jax.random.fold_in(_tk, 803), (256, 1), jnp.float32)
        b_top1 = jnp.zeros((512,), jnp.float32)
        b_top2 = jnp.zeros((256,), jnp.float32)
        return (dense_ctx, ids, tbl_0, tbl_1, tbl_2, tbl_3, tbl_4, tbl_5, tbl_6, tbl_7, tbl_8, tbl_9, tbl_10, tbl_11, tbl_12, tbl_13, tbl_14, tbl_15, tbl_16, tbl_17, tbl_18, tbl_19, tbl_20, tbl_21, tbl_22, tbl_23, tbl_24, tbl_25, tbl_26, tbl_27, tbl_28, tbl_29, tbl_30, tbl_31, W_top1, b_top1, W_top2, b_top2, W_top3)
    dense_ctx, ids, tbl_0, tbl_1, tbl_2, tbl_3, tbl_4, tbl_5, tbl_6, tbl_7, tbl_8, tbl_9, tbl_10, tbl_11, tbl_12, tbl_13, tbl_14, tbl_15, tbl_16, tbl_17, tbl_18, tbl_19, tbl_20, tbl_21, tbl_22, tbl_23, tbl_24, tbl_25, tbl_26, tbl_27, tbl_28, tbl_29, tbl_30, tbl_31, W_top1, b_top1, W_top2, b_top2, W_top3 = _rec_inputs()

    def _L0_rec_setup():
        import jax, jax.numpy as jnp
        import numpy as np
        FIELDS = 32
        EMBED = 64
        BATCH = 1024
        PAIR = FIELDS * (FIELDS - 1) // 2

        def _pair_ids(fields):
            pairs = np.array([(i, j) for i in range(fields - 1) for j in range(i + 1, fields)], dtype=np.int32)
            return (jnp.asarray(pairs[:, 0]), jnp.asarray(pairs[:, 1]))
        key = jax.random.key(seed)
        k1, k2 = jax.random.split(key)
        inputs = jax.random.normal(k1, (BATCH, FIELDS, EMBED), dtype=jnp.float32)
        w = 0.05 * jax.random.normal(k2, (PAIR, EMBED, EMBED), dtype=jnp.float32)
        return {'inputs': inputs, 'w': w}
    _L0_rec_all = _L0_rec_setup()
    _L0_rec_in = {k: v for k, v in _L0_rec_all.items() if k in ('w',)}
    del _L0_rec_all
    return {'dense_ctx': dense_ctx, 'ids': ids, 'tbl_0': tbl_0, 'tbl_1': tbl_1, 'tbl_2': tbl_2, 'tbl_3': tbl_3, 'tbl_4': tbl_4, 'tbl_5': tbl_5, 'tbl_6': tbl_6, 'tbl_7': tbl_7, 'tbl_8': tbl_8, 'tbl_9': tbl_9, 'tbl_10': tbl_10, 'tbl_11': tbl_11, 'tbl_12': tbl_12, 'tbl_13': tbl_13, 'tbl_14': tbl_14, 'tbl_15': tbl_15, 'tbl_16': tbl_16, 'tbl_17': tbl_17, 'tbl_18': tbl_18, 'tbl_19': tbl_19, 'tbl_20': tbl_20, 'tbl_21': tbl_21, 'tbl_22': tbl_22, 'tbl_23': tbl_23, 'tbl_24': tbl_24, 'tbl_25': tbl_25, 'tbl_26': tbl_26, 'tbl_27': tbl_27, 'tbl_28': tbl_28, 'tbl_29': tbl_29, 'tbl_30': tbl_30, 'tbl_31': tbl_31, 'W_top1': W_top1, 'b_top1': b_top1, 'W_top2': W_top2, 'b_top2': b_top2, 'W_top3': W_top3, 'L0_rec_w': _L0_rec_in['w']}

def reference(dense_ctx, ids, tbl_0, tbl_1, tbl_2, tbl_3, tbl_4, tbl_5, tbl_6, tbl_7, tbl_8, tbl_9, tbl_10, tbl_11, tbl_12, tbl_13, tbl_14, tbl_15, tbl_16, tbl_17, tbl_18, tbl_19, tbl_20, tbl_21, tbl_22, tbl_23, tbl_24, tbl_25, tbl_26, tbl_27, tbl_28, tbl_29, tbl_30, tbl_31, W_top1, b_top1, W_top2, b_top2, W_top3, L0_rec_w):
    import jax
    import jax.numpy as jnp

    def _L0_rec_ref(inputs, w):
        import jax, jax.numpy as jnp
        import numpy as np
        FIELDS = 32
        EMBED = 64
        BATCH = 1024
        PAIR = FIELDS * (FIELDS - 1) // 2

        def _pair_ids(fields):
            pairs = np.array([(i, j) for i in range(fields - 1) for j in range(i + 1, fields)], dtype=np.int32)
            return (jnp.asarray(pairs[:, 0]), jnp.asarray(pairs[:, 1]))
        ids_x, ids_y = _pair_ids(FIELDS)
        p = inputs[:, ids_x, :]
        q = inputs[:, ids_y, :]
        pw = jnp.einsum('bpi,pij->bpj', p, w)
        out = jnp.einsum('bpj,bpj->bp', pw, q)
        return out
    e = jnp.stack([tbl_0[ids[:, 0]], tbl_1[ids[:, 1]], tbl_2[ids[:, 2]], tbl_3[ids[:, 3]], tbl_4[ids[:, 4]], tbl_5[ids[:, 5]], tbl_6[ids[:, 6]], tbl_7[ids[:, 7]], tbl_8[ids[:, 8]], tbl_9[ids[:, 9]], tbl_10[ids[:, 10]], tbl_11[ids[:, 11]], tbl_12[ids[:, 12]], tbl_13[ids[:, 13]], tbl_14[ids[:, 14]], tbl_15[ids[:, 15]], tbl_16[ids[:, 16]], tbl_17[ids[:, 17]], tbl_18[ids[:, 18]], tbl_19[ids[:, 19]], tbl_20[ids[:, 20]], tbl_21[ids[:, 21]], tbl_22[ids[:, 22]], tbl_23[ids[:, 23]], tbl_24[ids[:, 24]], tbl_25[ids[:, 25]], tbl_26[ids[:, 26]], tbl_27[ids[:, 27]], tbl_28[ids[:, 28]], tbl_29[ids[:, 29]], tbl_30[ids[:, 30]], tbl_31[ids[:, 31]]], axis=1)
    z = _L0_rec_ref(e, L0_rec_w)
    z = z.reshape(z.shape[0], -1)
    h = jnp.concatenate([z, dense_ctx], axis=1)
    h = jnp.maximum(h @ W_top1 + b_top1, 0.0)
    h = jnp.maximum(h @ W_top2 + b_top2, 0.0)
    y = h @ W_top3
    return y

_drawn_inputs = setup_inputs


def setup_inputs(seed=0):
    import zlib

    import numpy as np

    out = dict(_drawn_inputs(seed))
    spreads = {'b_top1': (0.0, 0.1), 'b_top2': (0.0, 0.1)}
    factors = {'tbl_0': 6.385,
     'tbl_1': 6.276,
     'tbl_2': 6.088,
     'tbl_3': 6.251,
     'tbl_4': 4.962,
     'tbl_5': 6.122,
     'tbl_6': 5.944,
     'tbl_7': 5.289,
     'tbl_8': 5.962,
     'tbl_9': 5.735,
     'tbl_10': 6.242,
     'tbl_11': 5.129,
     'tbl_12': 5.207,
     'tbl_13': 5.271,
     'tbl_14': 5.662,
     'tbl_15': 5.547,
     'tbl_16': 5.424,
     'tbl_17': 6.175,
     'tbl_18': 5.146,
     'tbl_19': 5.368,
     'tbl_20': 5.792,
     'tbl_21': 5.583,
     'tbl_22': 5.76,
     'tbl_23': 6.19,
     'tbl_24': 6.027,
     'tbl_25': 5.515,
     'tbl_26': 5.587,
     'tbl_27': 6.062,
     'tbl_28': 5.813,
     'tbl_29': 5.884,
     'tbl_30': 5.893,
     'tbl_31': 5.97}
    for name, (base, spread) in spreads.items():
        noise = np.random.default_rng([zlib.crc32(name.encode()), seed]).standard_normal(out[name].shape)
        drawn = base * np.exp(spread * noise) if base else spread * noise
        out[name] = jnp.asarray(drawn.astype(out[name].dtype))
    for name, factor in factors.items():
        out[name] = (out[name] * factor).astype(out[name].dtype)
    return out
```

```python
from contextlib import ExitStack

import numpy as np

import concourse.bass as bass
from concourse import mybir

F32 = mybir.dt.float32
F32R = mybir.dt.float32r
I32 = mybir.dt.int32
U32 = mybir.dt.uint32
ALU = mybir.AluOpType
ACT = mybir.ActivationFunctionType

P = 128
FIELDS = 32
EMB = 64
BATCH = 512
BCH = BATCH // P
DENSE = 16
H1, H2 = 512, 256
N1, N2 = H1 // P, H2 // P

BLOCKS = []
for _x in range(1, FIELDS):
    _ms = list(range((_x + 1) // 2))
    if len(BLOCKS) % 2:
        _last = BLOCKS[-1][1]
        _ms.remove(_last)
        _ms.insert(0, _last)
    BLOCKS += [(_x, _m) for _m in _ms]
NB = len(BLOCKS)
QUADS = NB // 4
ZCH = QUADS // 16
CH = 16
WCH = NB // CH
WCOLS = CH * P
STEPS_PER_W = CH // 4
assert NB == 256 and ZCH * P == FIELDS * (FIELDS - 1) // 2 + DENSE

HALVED = 16
HB = BATCH // 2
PARTS = [(x, b, HB) for b in (0, HB) for x in range(HALVED)] + [(x, 0, BATCH) for x in range(HALVED, FIELDS)]
NP = len(PARTS)
NH = sum(x < HALVED for x, _ in BLOCKS)
STEPS = [(n, b, HB) for b in (0, HB) for n in range(0, NH, 4)] + [(n, 0, BATCH) for n in range(NH, NB, 4)]
assert NH == 64


def part_of(n, b):
    x = BLOCKS[n][0]
    return next(j for j, p in enumerate(PARTS) if p[:2] == (x, b))


FIRST, LAST = {}, {}
for _t, (_n, _b, _) in enumerate(STEPS):
    for _i in range(4):
        FIRST.setdefault(part_of(_n + _i, _b), _t)
        LAST[part_of(_n + _i, _b)] = _t


def splits(j):
    return sum(x > 0 for x, _, _ in PARTS[:j + 1])


def half(n):
    x, m = BLOCKS[n]
    return 2 * m + 1 == x


def z_row(n, r):
    q, c = divmod(n, 4)
    return (q // 16) * P + 32 * c + 2 * (q % 16) + r


ER = 10
XR = 4
RAWR = 3
WSR = 7
AHEAD = 2
L_AHEAD = 3
W_AFTER = [1, 3, 6]
H_START = 2
H_AHEAD = 2
L_DVE = 6
L_POOL_FROM = 33

PREP = {0: -1}
for _j in range(1, NP):
    PREP[_j] = max(-1, FIRST.get(_j, FIRST.get(_j + 1)) - AHEAD, LAST.get(_j - XR, -1), PREP[_j - 1])
    assert PREP[_j] < FIRST.get(_j, NB)
PREPS = {t: [j for j in range(NP) if PREP[j] == t] for t in range(-1, len(STEPS))}

W_FIRST = [min(t for t, s in enumerate(STEPS) if s[0] // CH == k) for k in range(WCH)]
W_LAST = [max(t for t, s in enumerate(STEPS) if s[0] // CH == k) for k in range(WCH)]
L_PIECES = {t: [] for t in range(-1, len(STEPS))}
for _i in range(STEPS_PER_W * (L_DVE - 1)):
    _k = 1 + _i // STEPS_PER_W
    L_PIECES[max(0, min(_i, W_FIRST[_k] - L_AHEAD))].append((_k, _i % STEPS_PER_W))
H_AT = [-1]
for _k in range(1, WCH):
    _t = min(t for t in L_PIECES if (_k, 0) in L_PIECES[t]) if _k < L_DVE else W_FIRST[_k] - 9
    H_AT.append(max(-1, _t - H_AHEAD, H_AT[-1], W_LAST[_k - WSR] + 1 if _k >= WSR else -1))
H_CHUNKS = {t: [k for k in range(WCH) if H_AT[k] == t] for t in range(-1, len(STEPS))}
Z_LAST = [max(t for t, s in enumerate(STEPS) if s[0] // 64 == c) for c in range(ZCH)]
L_POOL = {j: [] for j in range(NP)}
for _k in range(L_DVE, WCH):
    L_POOL[min(NP - 1, L_POOL_FROM + 2 * (_k - L_DVE))].append(_k)


def dlrm_tower(nc, tables, ids, w, dense, w1, b1, w2, b2, w3, ident, out):
    with ExitStack() as ctx:
        def sb(name, shape, dt=F32):
            return ctx.enter_context(nc.sbuf_tensor(name, shape, dt))

        def ps(name, shape):
            return ctx.enter_context(nc.psum_tensor(name, shape, F32))

        def sem(name):
            return ctx.enter_context(nc.semaphore(name))

        idx = sb("idx", [P, BCH, FIELDS], I32)
        identity = sb("identity", [P, P])
        emb = sb("emb", [P, ER, BCH, 2, EMB])
        eT = sb("eT", [P, FIELDS // 2, BATCH])
        xh = sb("xh", [P, XR, BATCH], F32R)
        xl = sb("xl", [P, XR, BATCH], F32R)
        raw = sb("raw", [P, RAWR, WCOLS])
        ws = sb("ws", [P, WSR, WCOLS], F32R)
        prod = sb("prod", [P, 2, 4, BATCH])
        select = sb("select", [P, 64])
        zT = sb("zT", [P, ZCH, BATCH])
        denseT = sb("denseT", [P, ZCH, BATCH])
        w1s = sb("w1s", [P, ZCH, H1])
        w2s = sb("w2s", [P, N1, H2])
        w3s = sb("w3s", [P, N2])
        b1s = sb("b1s", [P, N1])
        b2s = sb("b2s", [P, N2])
        h1 = prod[:, len(STEPS) % 2, :, :]
        h2 = sb("h2", [P, N2, BATCH])
        y = sb("y", [1, BATCH])

        pu = ps("pu", [P, 4, BATCH])
        pt = ps("pt", [P, 2, BATCH])
        pz = ps("pz", [P, 2, BATCH])

        s_idx = sem("idx_in")
        s_ident = sem("identity_in")
        s_emb = [sem(f"emb_in{j}") for j in range(NP)]
        s_raw = [sem(f"raw_in{i}") for i in range(RAWR)]
        s_dense = [sem(f"dense_in{c}") for c in range(ZCH)]
        s_mlp = sem("mlp_in")
        zeroed = sem("select_zeroed")
        selected = sem("select_ready")
        wh_ready = sem("w_high_ready")
        wl_dve = sem("w_low_by_vector")
        wl_pool = sem("w_low_by_gpsimd")
        e_twice = sem("e_twice")
        xt_ready = sem("transposed")
        xh_ready = sem("x_high_ready")
        et_ready = sem("eT_ready")
        xl_ready = sem("x_low_ready")
        u_ready = sem("u_ready")
        mult_done = sem("mult_done")
        sum_done = sem("sum_done")
        z_out = sem("z_in_sbuf")
        h1_ready = sem("h1_ready")
        h1_act = sem("h1_by_scalar")
        h1_dve = sem("h1_by_vector")
        h2_ready = sem("h2_ready")
        h2_act = sem("h2_by_scalar")
        h2_dve = sem("h2_by_vector")
        y_ready = sem("y_ready")
        y_out = sem("y_in_sbuf")
        stored = sem("stored")

        block = ctx.enter_context(nc.Block())

        def wl_wait(eng, k):
            if k < L_DVE:
                eng.wait_ge(wl_dve, k + 1)
            else:
                eng.wait_ge(wl_pool, k + 1 - L_DVE)

        def u_of(t, i):
            cols = STEPS[t][2]
            if cols == HB:
                return pu[:, (2 * t + i) % 4, :].rearrange("p (n b) -> p n b", n=2)
            return pu[:, 2 * i:2 * i + 2, :]

        def layer1(n):
            return pt[:, n, :] if n < 2 else pu[:, n, :]

        @block.sync
        def _(sp):
            sp.dma_start(idx[:], ids).then_inc(s_idx, 16)
            sp.dma_start(identity[:], ident).then_inc(s_ident, 16)
            for k in range(WCH):
                if 1 <= k <= RAWR:
                    sp.wait_ge(s_emb[W_AFTER[k - 1]], 16 * (HB // P))
                if k >= RAWR:
                    sp.wait_ge(wh_ready, k - RAWR + 1)
                    wl_wait(sp, k - RAWR)
                for h in range(2):
                    sp.dma_start(raw[EMB * h:EMB * (h + 1), k % RAWR, :],
                                 w[:, k * WCOLS:(k + 1) * WCOLS]).then_inc(s_raw[k % RAWR], 16)
                if k >= 4 and (k - 4) % 3 == 0 and (k - 4) // 3 < ZCH:
                    c = (k - 4) // 3
                    sp.dma_start(denseT[:, c, :], dense[:, c, :]).then_inc(s_dense[c], 16)
                if k >= WCH - ZCH:
                    c = k - (WCH - ZCH)
                    sp.dma_start(w1s[:, c, :], w1[:, c, :]).then_inc(s_mlp, 16)
            sp.dma_start(w2s[:], w2).then_inc(s_mlp, 16)
            sp.dma_start(w3s[:], w3).then_inc(s_mlp, 16)
            sp.dma_start(b1s[:], b1).then_inc(s_mlp, 16)
            sp.dma_start(b2s[:], b2).then_inc(s_mlp, 16)
            sp.wait_ge(y_out, 1)
            sp.dma_start(out, y[:]).then_inc(stored, 16)
            sp.wait_ge(stored, 16)

        def low_part(eng, k, a, b):
            high = ws[EMB:P, k % WSR, a:b]
            return eng.tensor_tensor(high, raw[EMB:P, k % RAWR, a:b], high.bitcast(F32), ALU.subtract)

        @block.gpsimd
        def _(pool):
            pool.wait_ge(s_idx, 16)
            landed = 0
            for j, (x, b, n) in enumerate(PARTS):
                if j >= ER:
                    pool.wait_ge(xt_ready, j - ER + 1)
                for c in range(b // P, (b + n) // P):
                    nc.gpsimd.indirect_dma_start(
                        out=emb[:, j % ER, c - b // P, 0, :], out_offset=None, in_=tables[x],
                        in_offset=bass.IndirectOffsetOnAxis(ap=idx[:, c, x:x + 1].bitcast(U32), axis=0),
                    ).then_inc(s_emb[j], 16)
                if L_POOL[j]:
                    for i in range(landed, j + 1):
                        pool.wait_ge(s_emb[i], 16 * (PARTS[i][2] // P))
                    landed = j + 1
                for k in L_POOL[j]:
                    pool.wait_ge(wh_ready, k + 1)
                    low_part(nc.gpsimd, k, 0, WCOLS).then_inc(wl_pool, 1)
                if L_POOL[j] and j < NP - 1:
                    pool.wait_ge(wl_pool, L_POOL[j][-1] - L_DVE + 1)

        @block.scalar
        def _(act):
            def split_w(k):
                act.wait_ge(s_raw[k % RAWR], 32 * (k // RAWR + 1))
                if k >= WSR:
                    act.wait_ge(u_ready, 2 * (W_LAST[k - WSR] + 1))
                nc.scalar.copy(ws[:, k % WSR, :], raw[:, k % RAWR, :]).then_inc(wh_ready, 1)

            def twice(j):
                n = PARTS[j][2] // P
                act.wait_ge(s_emb[j], 16 * n)
                nc.scalar.copy(emb[:, j % ER, 0:n, 1, :], emb[:, j % ER, 0:n, 0, :]).then_inc(e_twice, 1)

            def prepare(j):
                x, b, n = PARTS[j]
                act.wait_ge(xt_ready, j + 1)
                if x > 0:
                    if LAST.get(j - XR, -1) >= 0:
                        act.wait_ge(u_ready, 2 * (LAST[j - XR] + 1))
                    nc.scalar.copy(xh[:, j % XR, 0:n], pt[:, j % 2, 0:n]).then_inc(xh_ready, 1)
                h = slice(EMB * (x % 2), EMB * (x % 2) + EMB)
                nc.scalar.copy(eT[h, x // 2, b:b + n], pt[h, j % 2, 0:n]).then_inc(et_ready, 1)

            for t in range(-1, len(STEPS)):
                for k in H_CHUNKS[t]:
                    if t >= 0 or k == 0:
                        split_w(k)
                for j in PREPS[t]:
                    twice(j)
                    prepare(j)
                    if j == H_START:
                        for k in H_CHUNKS[-1][1:]:
                            split_w(k)

            act.wait_ge(s_mlp, (ZCH + 4) * 16)
            for n in range(0, N1, 2):
                act.wait_ge(h1_ready, n + 1)
                nc.scalar.activation(h1[:, n, :], layer1(n), ACT.Relu, bias=b1s[:, n:n + 1]).then_inc(h1_act, 1)
            for n in range(0, N2, 2):
                act.wait_ge(h2_ready, n + 1)
                nc.scalar.activation(h2[:, n, :], pu[:, n, :], ACT.Relu, bias=b2s[:, n:n + 1]).then_inc(h2_act, 1)
            act.wait_ge(y_ready, 1)
            nc.scalar.copy(y[:], pz[0:1, 0, :]).then_inc(y_out, 1)

        @block.vector
        def _(dve):
            nc.vector.memset(select[:], 0.0).then_inc(zeroed, 1)
            dve.wait_ge(zeroed, 1)
            nc.vector.memset(select[0:EMB, 30:31], 1.0).then_inc(selected, 1)
            nc.vector.memset(select[EMB:P, 31:32], 1.0).then_inc(selected, 1)

            def split_w(k, part, parts):
                dve.wait_ge(wh_ready, k + 1)
                n = WCOLS // parts
                i = low_part(nc.vector, k, part * n, (part + 1) * n)
                if part == parts - 1:
                    i.then_inc(wl_dve, 1)

            def prepare(j):
                n = PARTS[j][2]
                dve.wait_ge(xh_ready, splits(j))
                dve.wait_ge(et_ready, j + 1)
                nc.vector.tensor_tensor(xl[:, j % XR, 0:n], pt[:, j % 2, 0:n], xh[:, j % XR, 0:n].bitcast(F32),
                                        ALU.subtract).then_inc(xl_ready, 1)

            def multiply(t, i):
                n, b, cols = STEPS[t]
                n, pair = n + 2 * i, 2 * t + i
                (xa, ma), (xb, mb) = BLOCKS[n], BLOCKS[n + 1]
                dve.wait_ge(u_ready, pair + 1)
                dve.wait_ge(et_ready, part_of(n + 1, b) + 1)
                if t >= 2:
                    dve.wait_ge(sum_done, t - 1)
                if ma == mb:
                    e = eT[:, ma:ma + 1, b:b + cols].broadcast_to([P, 2, cols])
                else:
                    e = eT[:, ma:mb + 1:mb - ma, b:b + cols]
                nc.vector.tensor_tensor(prod[:, t % 2, 2 * i:2 * i + 2, 0:cols], u_of(t, i), e,
                                        ALU.mult).then_inc(mult_done, 1)

            def z_rows(c):
                dve.wait_ge(s_dense[c], 16)
                dve.wait_ge(sum_done, Z_LAST[c] + 1)
                nc.vector.tensor_tensor(zT[:, c, :], pz[:, c % 2, :], denseT[:, c, :],
                                        ALU.add).then_inc(z_out, 1)

            for j in PREPS[-1]:
                if j == 1:
                    split_w(0, 0, 1)
                if PARTS[j][0] > 0:
                    prepare(j)
            for t in range(len(STEPS)):
                multiply(t, 0)
                multiply(t, 1)
                for j in PREPS[t]:
                    if PARTS[j][0] > 0:
                        prepare(j)
                for k, i in L_PIECES[t]:
                    split_w(k, i, STEPS_PER_W)
                for c in range(ZCH - 1):
                    if t == Z_LAST[c] + 2:
                        z_rows(c)
            z_rows(ZCH - 1)
            for n in range(1, N1, 2):
                dve.wait_ge(h1_ready, n + 1)
                nc.vector.tensor_scalar(h1[:, n, :], layer1(n), b1s[:, n:n + 1], 0.0, ALU.add,
                                        ALU.max).then_inc(h1_dve, 1)
            for n in range(1, N2, 2):
                dve.wait_ge(h2_ready, n + 1)
                nc.vector.tensor_scalar(h2[:, n, :], pu[:, n, :], b2s[:, n:n + 1], 0.0, ALU.add,
                                        ALU.max).then_inc(h2_dve, 1)

        @block.tensor
        def _(pe):
            def transpose(j):
                pe.wait_ge(e_twice, j + 1)
                if j >= 2:
                    pe.wait_ge(et_ready, j - 1)
                    if splits(j - 2):
                        pe.wait_ge(xl_ready, splits(j - 2))
                for c in range(PARTS[j][2] // P):
                    i = nc.tensor.transpose(pt[:, j % 2, c * P:(c + 1) * P],
                                            emb[:, j % ER, c, :, :].rearrange("p t i -> p (t i)"), identity[:])
                i.then_inc(xt_ready, 1)

            def products(t):
                n0, b, cols = STEPS[t]
                if t in W_FIRST:
                    pe.wait_ge(wh_ready, n0 // CH + 1)
                    wl_wait(pe, n0 // CH)
                for i in range(2):
                    free = 2 * t + i + 1 - (4 if cols == HB else 2)
                    if free > 0:
                        pe.wait_ge(mult_done, free)
                    for a in range(2):
                        n = n0 + 2 * i + a
                        j = part_of(n, b)
                        if FIRST[j] == t:
                            pe.wait_ge(xh_ready, splits(j))
                            pe.wait_ge(xl_ready, splits(j))
                        k, at = n // CH, n % CH * P
                        weights = ws[:, k % WSR, at:at + P]
                        u = u_of(t, i)[:, a, :]
                        nc.tensor.matmul(u, weights, xh[:, j % XR, 0:cols], start=True, stop=False)
                        mm = nc.tensor.matmul(u, weights, xl[:, j % XR, 0:cols], start=False, stop=True)
                    mm.then_inc(u_ready, 1)

            def sums(t):
                n0, b, cols = STEPS[t]
                c, s = divmod(n0 // 4, 16)
                pe.wait_ge(mult_done, 2 * t + 2)
                if s == 0 and c >= 2:
                    pe.wait_ge(z_out, c - 1)
                for a in range(4):
                    k = EMB if half(n0 + a) else P
                    i = nc.tensor.matmul(pz[32 * a:32 * a + 32, c % 2, b:b + cols],
                                         select[0:k, 30 - 2 * s:62 - 2 * s],
                                         prod[0:k, t % 2, a, 0:cols], start=(s == 0), stop=(s == 15))
                i.then_inc(sum_done, 1)

            pe.wait_ge(s_ident, 16)
            pe.wait_ge(selected, 2)
            for j in PREPS[-1]:
                transpose(j)
            for t in range(len(STEPS)):
                products(t)
                for j in PREPS[t]:
                    transpose(j)
                if t >= 1:
                    sums(t - 1)

            def first_layer(n, chunks):
                for c in chunks:
                    i = nc.tensor.matmul(layer1(n), w1s[:, c, n * P:(n + 1) * P], zT[:, c, :],
                                         start=(c == 0), stop=(c == ZCH - 1))
                if c == ZCH - 1:
                    i.then_inc(h1_ready, 1)

            pe.wait_ge(s_mlp, (ZCH + 4) * 16)
            pe.wait_ge(z_out, ZCH - 1)
            pe.wait_ge(et_ready, NP)
            pe.wait_ge(xl_ready, splits(NP - 1))
            first_layer(0, range(ZCH - 1))
            first_layer(1, range(ZCH - 1))
            sums(len(STEPS) - 1)
            first_layer(2, range(ZCH - 1))
            pe.wait_ge(z_out, ZCH)
            for n in range(3):
                first_layer(n, [ZCH - 1])
            first_layer(3, range(ZCH))
            for c in range(N1):
                pe.wait_ge(h1_dve if c % 2 else h1_act, c // 2 + 1)
                for n in range(N2):
                    i = nc.tensor.matmul(pu[:, n, :], w2s[:, c, n * P:(n + 1) * P], h1[:, c, :],
                                         start=(c == 0), stop=(c == N1 - 1))
                    if c == N1 - 1:
                        i.then_inc(h2_ready, 1)
            for c in range(N2):
                pe.wait_ge(h2_dve if c % 2 else h2_act, c // 2 + 1)
                i = nc.tensor.matmul(pz[0:1, 0, :], w3s[:, c:c + 1], h2[:, c, :],
                                     start=(c == 0), stop=(c == N2 - 1))
            i.then_inc(y_ready, 1)


def kernel(**inputs):
    import concourse.bacc as bacc
    from concourse.bass_utils import run_bass_kernel_spmd

    w = np.asarray(inputs["L0_rec_w"])
    pair = {}
    for i in range(FIELDS - 1):
        for j in range(i + 1, FIELDS):
            pair[i, j] = len(pair)
    order = [pair[2 * m + (0 if half(n) else r), x] for n, (x, m) in enumerate(BLOCKS) for r in range(2)]
    w_blocks = np.ascontiguousarray(w[order].transpose(2, 0, 1).reshape(EMB, NB * P))

    rows = np.zeros(ZCH * P, np.int64)
    dense_rows = []
    for n, (x, m) in enumerate(BLOCKS):
        rows[z_row(n, 0)] = pair[2 * m, x]
        if half(n):
            rows[z_row(n, 1)] = len(pair) + len(dense_rows)
            dense_rows.append(z_row(n, 1))
        else:
            rows[z_row(n, 1)] = pair[2 * m + 1, x]
    w1 = np.asarray(inputs["W_top1"])[rows].reshape(ZCH, P, H1).transpose(1, 0, 2)
    dense = np.zeros((ZCH * P, BATCH), np.float32)
    dense[dense_rows] = np.asarray(inputs["dense_ctx"]).T
    dense = dense.reshape(ZCH, P, BATCH).transpose(1, 0, 2)

    arrays = {
        "ids": np.asarray(inputs["ids"]).reshape(BCH, P, FIELDS).transpose(1, 0, 2),
        "w": w_blocks,
        "dense": dense,
        "w1": w1,
        "b1": np.asarray(inputs["b_top1"]).reshape(N1, P).T,
        "w2": np.asarray(inputs["W_top2"]).reshape(N1, P, H2).transpose(1, 0, 2),
        "b2": np.asarray(inputs["b_top2"]).reshape(N2, P).T,
        "w3": np.asarray(inputs["W_top3"]).reshape(N2, P).T,
        "ident": np.eye(P, dtype=np.float32),
    }
    for f in range(FIELDS):
        arrays[f"tbl_{f}"] = np.asarray(inputs[f"tbl_{f}"])
    arrays = {f"in_{k}": np.ascontiguousarray(v) for k, v in arrays.items()}

    nc = bacc.Bacc("TRN2", target_bir_lowering=False, num_devices=1)
    aps = {k[3:]: nc.dram_tensor(k, v.shape, mybir.dt.from_np(v.dtype), kind="ExternalInput").ap()
           for k, v in arrays.items()}
    out = nc.dram_tensor("out_y", (BATCH, 1), F32, kind="ExternalOutput").ap()
    dlrm_tower(nc, [aps[f"tbl_{f}"] for f in range(FIELDS)], aps["ids"], aps["w"], aps["dense"],
               aps["w1"], aps["b1"], aps["w2"], aps["b2"], aps["w3"], aps["ident"],
               out.rearrange("b o -> o b"))
    r = run_bass_kernel_spmd(nc, [arrays], core_ids=[0])
    return r.results[0]["out_y"]
```
